# Optimizing a Trainium2 kernel written in Bass

```python
import numpy as np
import jax
import jax.numpy as jnp

def _softmax(x, axis=-1):
    return jax.nn.softmax(x, axis=axis)

def _gelu(x):
    return jax.nn.gelu(x, approximate=True)

def _silu(x):
    return jax.nn.silu(x)

def _sigmoid(x):
    return jax.nn.sigmoid(x)

def _layernorm(x, axis=-1, eps=1e-05):
    m = jnp.mean(x, axis=axis, keepdims=True)
    v = jnp.var(x, axis=axis, keepdims=True)
    return (x - m) / jnp.sqrt(v + eps)

def _scatter_add(tgt, idx, src, axis=0):
    return tgt.at[idx].add(src)

def _segment_sum(src, seg, n):
    return jax.ops.segment_sum(src, seg, n)
kernel_name = 'mk_seq_postln_d1_jaxref_r4_f91004'

def setup_inputs(seed: int=0):
    np.random.seed(seed)
    _w = jnp.asarray

    def _L0_attn_setup():
        import jax, jax.numpy as jnp
        import numpy as np
        B_SZ, L, D, N, R = (2, 512, 512, 128, 128)
        key = jax.random.key(seed)
        ks = jax.random.split(key, 8)
        s = lambda k, shape: jax.random.normal(k, shape, jnp.float32) * 0.02
        return {'x': jax.random.normal(ks[0], (B_SZ, L, D), jnp.float32), 'norm_w': jnp.ones((D,), jnp.float32), 'select_proj_w': s(ks[1], (D, D)), 'select_proj_b': jnp.zeros((D,), jnp.float32), 'select_gate': jnp.ones((D,), jnp.float32), 'x_proj_w': s(ks[2], (R + 2 * N, D)), 'dt_proj_w': s(ks[3], (D, R)), 'dt_proj_b': jnp.zeros((D,), jnp.float32), 'A_log': s(ks[4], (D, N)), 'D_param': jnp.ones((D,), jnp.float32), 'out_proj_w': s(ks[5], (D, D))}
    _L0_attn_in = _L0_attn_setup()

    def _L0_ffn_setup():
        import jax, jax.numpy as jnp
        import numpy as np
        DIM_IN = 512
        DIM_HIDDEN = 2048
        key = jax.random.key(seed)
        k_x, k_g, k_u, k_d = jax.random.split(key, 4)
        s_in = 1.0 / np.sqrt(DIM_IN)
        s_hid = 1.0 / np.sqrt(DIM_HIDDEN)
        x = jax.random.normal(k_x, (4, 512, DIM_IN), dtype=jnp.float32)
        w_gate = jax.random.uniform(k_g, (DIM_HIDDEN, DIM_IN), jnp.float32, -s_in, s_in)
        w_up = jax.random.uniform(k_u, (DIM_HIDDEN, DIM_IN), jnp.float32, -s_in, s_in)
        w_down = jax.random.uniform(k_d, (DIM_IN, DIM_HIDDEN), jnp.float32, -s_hid, s_hid)
        return {'x': x, 'w_gate': w_gate, 'w_up': w_up, 'w_down': w_down}
    _L0_ffn_in = _L0_ffn_setup()
    _d = {'L0_attn_x': _L0_attn_in['x'], 'L0_attn_norm_w': _L0_attn_in['norm_w'], 'L0_attn_select_proj_w': _L0_attn_in['select_proj_w'], 'L0_attn_select_proj_b': _L0_attn_in['select_proj_b'], 'L0_attn_select_gate': _L0_attn_in['select_gate'], 'L0_attn_x_proj_w': _L0_attn_in['x_proj_w'], 'L0_attn_dt_proj_w': _L0_attn_in['dt_proj_w'], 'L0_attn_dt_proj_b': _L0_attn_in['dt_proj_b'], 'L0_attn_A_log': _L0_attn_in['A_log'], 'L0_attn_D_param': _L0_attn_in['D_param'], 'L0_attn_out_proj_w': _L0_attn_in['out_proj_w'], 'L0_ffn_w_gate': _L0_ffn_in['w_gate'], 'L0_ffn_w_up': _L0_ffn_in['w_up'], 'L0_ffn_w_down': _L0_ffn_in['w_down']}
    _x0 = _d['L0_attn_x']
    _d['L0_attn_x'] = jax.random.normal(jax.random.fold_in(jax.random.key(seed), 1), (2, 1024, 512), dtype=_x0.dtype)
    del _x0
    return _d

def reference(L0_attn_x, L0_attn_norm_w, L0_attn_select_proj_w, L0_attn_select_proj_b, L0_attn_select_gate, L0_attn_x_proj_w, L0_attn_dt_proj_w, L0_attn_dt_proj_b, L0_attn_A_log, L0_attn_D_param, L0_attn_out_proj_w, L0_ffn_w_gate, L0_ffn_w_up, L0_ffn_w_down):

    def _L0_attn_ref(x, norm_w, select_proj_w, select_proj_b, select_gate, x_proj_w, dt_proj_w, dt_proj_b, A_log, D_param, out_proj_w):
        import jax, jax.numpy as jnp
        import numpy as np
        B_SZ, L, D, N, R = (2, 512, 512, 128, 128)
        xn = x * jax.lax.rsqrt(jnp.mean(x * x, axis=-1, keepdims=True) + 1e-06) * norm_w
        mask = jax.nn.sigmoid((xn @ select_proj_w.T + select_proj_b) * select_gate)
        xn = xn * mask
        xp = xn @ x_proj_w.T
        delta = xp[..., :R]
        B_ssm = xp[..., R:R + N]
        C_ssm = xp[..., R + N:]
        delta = jax.nn.softplus(delta @ dt_proj_w.T + dt_proj_b)
        A = -jnp.exp(A_log)

        def step(h, inp):
            dt, bt, ct, xt = inp
            h = jnp.exp(dt[:, :, None] * A) * h + (dt * xt)[:, :, None] * bt[:, None, :]
            y = jnp.einsum('bdn,bn->bd', h, ct)
            return (h, y)
        h0 = jnp.zeros((x.shape[0], D, N), x.dtype)
        xs = (jnp.moveaxis(delta, 1, 0), jnp.moveaxis(B_ssm, 1, 0), jnp.moveaxis(C_ssm, 1, 0), jnp.moveaxis(xn, 1, 0))
        _, ys = jax.lax.scan(step, h0, xs)
        y = jnp.moveaxis(ys, 0, 1)
        return (y + x * D_param) @ out_proj_w.T

    def _L0_ffn_ref(x, w_gate, w_up, w_down):
        import jax, jax.numpy as jnp
        import numpy as np
        DIM_IN = 512
        DIM_HIDDEN = 2048
        gate = jnp.einsum('bsd,hd->bsh', x, w_gate)
        up = jnp.einsum('bsd,hd->bsh', x, w_up)
        gated = jax.nn.silu(gate) * up
        return jnp.einsum('bsh,dh->bsd', gated, w_down)
    x = L0_attn_x
    x = _layernorm(x + _L0_attn_ref(x, L0_attn_norm_w, L0_attn_select_proj_w, L0_attn_select_proj_b, L0_attn_select_gate, L0_attn_x_proj_w, L0_attn_dt_proj_w, L0_attn_dt_proj_b, L0_attn_A_log, L0_attn_D_param, L0_attn_out_proj_w), axis=-1)
    x = _layernorm(x + _L0_ffn_ref(x, L0_ffn_w_gate, L0_ffn_w_up, L0_ffn_w_down), axis=-1)
    return x

_drawn_inputs = setup_inputs


def setup_inputs(seed=0):
    import zlib

    import numpy as np

    out = dict(_drawn_inputs(seed))
    spreads = {'L0_attn_norm_w': (1.0, 0.2),
     'L0_attn_select_proj_b': (0.0, 0.8),
     'L0_attn_select_gate': (1.0, 0.6),
     'L0_attn_dt_proj_b': (0.0, 0.8),
     'L0_attn_D_param': (1.0, 0.2)}
    factors = {'L0_attn_dt_proj_w': 8.0, 'L0_attn_A_log': 38.692}
    for name, (base, spread) in spreads.items():
        noise = np.random.default_rng([zlib.crc32(name.encode()), seed]).standard_normal(out[name].shape)
        drawn = base * np.exp(spread * noise) if base else spread * noise
        out[name] = jnp.asarray(drawn.astype(out[name].dtype))
    for name, factor in factors.items():
        out[name] = (out[name] * factor).astype(out[name].dtype)
    return out
```

```python
from contextlib import ExitStack

import concourse.bass as bass
from concourse import mybir

BATCH, SEQ, D, N, R, HID = 2, 1024, 512, 128, 128, 2048
P = 128
KB = D // P
TOK = BATCH * SEQ
TC = 512
CHUNKS = TOK // TC
PER_SEQ = SEQ // TC
HB = HID // P
XP = R + 2 * N
NV = 5
ROW_RING = 4
W_RING = 2
WT = 2 * KB * P


def pool_blocks(n):
    return 1 + (n % 3 == 0)


class Counter:

    def __init__(self, sem):
        self.sem, self.value = sem, 0


def build(nc, xT, vecs, sel_wT, xproj_wT, dt_wT, out_wT, A_log, gu_w, down_w, outT):
    f32 = mybir.dt.float32
    ALU = mybir.AluOpType
    ACT = mybir.ActivationFunctionType

    ctx = ExitStack()
    with ctx:
        def sb(name, shape):
            return ctx.enter_context(nc.sbuf_tensor(name, shape, f32))

        def ps(name, shape):
            return ctx.enter_context(nc.psum_tensor(name, shape, f32))

        ident = sb("ident", [P, P])
        mean_mat = sb("mean_mat", [P, P])
        one = sb("one", [P, 1])
        eps_rms = sb("eps_rms", [P, 1])
        eps_ln = sb("eps_ln", [P, 1])
        vec = sb("vec", [P, NV, KB])
        neg_gate = sb("neg_gate", [P, KB])
        neg_gate_bias = sb("neg_gate_bias", [P, KB])
        A = sb("A", [P, KB, N])
        w_sel = sb("w_sel", [P, KB, D])
        w_xp = sb("w_xp", [P, KB, XP])
        w_dt = sb("w_dt", [P, D])
        w_out = sb("w_out", [P, KB, D])
        carry = sb("carry", [P, N, KB])
        dt = [sb(f"dt{i}", [P, KB, TC]) for i in range(2)]
        u = [sb(f"u{i}", [P, KB, TC]) for i in range(2)]
        b_row = sb("b_row", [P, ROW_RING, TC])
        c_row = sb("c_row", [P, ROW_RING, TC])
        b = [sb(f"b{i}", [P, KB, TC]) for i in range(2)]
        h = [sb(f"h{i}", [P, KB, TC]) for i in range(2)]
        z = [sb(f"z{i}", [P, KB, TC]) for i in range(2)]
        rinv = sb("rinv", [P, TC])
        xp_out = [sb(f"xp_out{i}", [P, TC]) for i in range(2)]
        tmp = [sb(f"tmp{i}", [P, TC]) for i in range(3)]
        v = sb("v", [P, KB, TC])
        gated = sb("gated", [P, HB, TC])
        ymod = gated[:, 0:KB, :]
        w_ring = sb("w_ring", [P, W_RING, WT])

        y_ps = ps("y_ps", [P, KB, TC])
        a_ps = ps("a_ps", [P, 2, TC])
        c_ps = ps("c_ps", [P, TC])
        work = ps("work", [P, TC])

        bc_scratch = nc.dram_tensor("bc_scratch", [CHUNKS, 2, N, TC], f32, kind="Internal").ap()

        queues = {e: [] for e in ("sync", "scalar", "vector", "gpsimd", "tensor")}
        SP, SC, VE, GP, PE = queues.keys()
        waited = {}
        counters = {}

        def counter(name):
            if name not in counters:
                counters[name] = Counter(ctx.enter_context(nc.semaphore(name)))
            return counters[name]

        def wait(engine, *points):
            for point in points:
                if point is None:
                    continue
                c, value = point
                if waited.get((engine, c), 0) < value:
                    waited[engine, c] = value
                    queues[engine].append(lambda e, s=c.sem, n=value: e.wait_ge(s, n))

        def do(engine, name, issue, by=1):
            c = counter(name)
            c.value += by
            queues[engine].append(lambda e: issue(e).then_inc(c.sem, by))
            return c, c.value

        def quiet(engine, issue):
            queues[engine].append(lambda e: issue(e))

        def dma(name, dst, src):
            return do(SP, name, lambda e: e.dma_start(dst, src), 16)

        def act(name, dst, src, func, **kw):
            return do(SC, name, lambda e: e.activation(dst, src, func, **kw))

        def over_blocks(row, blocks=KB):
            return row.unsqueeze(1).to_broadcast([P, blocks, TC])

        quiet(SC, lambda e: e.preload_act_table_set("natural_log_exp_and_others"))
        vec_in = dma("d_vec", vec[:, :, :], vecs)
        alog_in = dma("d_alog", A[:, :, :], A_log.rearrange("(k p) n -> p k n", p=P))
        wsel_in = dma("d_wsel", w_sel[:, :, :], sel_wT.rearrange("(k p) m -> p k m", p=P))
        wxp_in = dma("d_wxp", w_xp[:, :, :], xproj_wT.rearrange("(k p) m -> p k m", p=P))
        wdt_in = dma("d_wdt", w_dt[:, :], dt_wT)
        wout_in = dma("d_wout", w_out[:, :, :], out_wT.rearrange("(k p) m -> p k m", p=P))
        do(VE, "consts", lambda e: e.memset(mean_mat[:, :], 1.0 / D))
        do(VE, "consts", lambda e: e.memset(one[:, :], 1.0))
        do(VE, "consts", lambda e: e.memset(eps_rms[:, :], 1e-6))
        consts = do(VE, "consts", lambda e: e.memset(eps_ln[:, :], 1e-5))
        zeroed = do(GP, "ident", lambda e: e.memset(ident[:, :], 0.0))
        wait(GP, zeroed)
        ident_done = do(GP, "ident", lambda e: e.affine_select(
            out=ident[:, :], in_=ident[:, :], compare_op=ALU.not_equal, fill=1.0, base=0,
            pattern=[[-1, P]], channel_multiplier=1))
        norm_w, sel_b, sel_g, dt_b, d_skip = (vec[:, i, :] for i in range(NV))
        wait(VE, vec_in)
        p = do(VE, "v_small", lambda e: e.tensor_scalar(neg_gate[:, :], sel_g, -1.0, None, ALU.mult))
        wait(VE, p)
        gates = do(VE, "v_small", lambda e: e.tensor_tensor(neg_gate_bias[:, :], neg_gate[:, :], sel_b, ALU.mult))
        wait(SC, alog_in)
        p = act("a_small", A[:, :, :], A[:, :, :], ACT.Exp)
        wait(VE, p)
        A_ready = do(VE, "v_small", lambda e: e.tensor_scalar(A[:, :, :], A[:, :, :], -1.0, None, ALU.mult))

        free = {"work": None, "dt": [None, None], "u": [None, None], "tmp": [None] * 3,
                "xp_out": [None, None], "rinv": None, "gated": None, "v": None,
                "w_ring": [None] * W_RING}
        loaded_tiles = [0]

        def project(parts, first, last):
            if first:
                wait(PE, free["work"])
            for i, (w, x) in enumerate(parts):
                s, t = first and i == 0, last and i == len(parts) - 1
                issue = (lambda e, w=w, x=x, s=s, t=t: e.matmul(work[:, :], w, x, start=s, stop=t))
                if i == len(parts) - 1:
                    return do(PE, "pe_work", issue)
                quiet(PE, issue)

        ready = {}

        def prepare(c):
            U, T = u[c % 2], dt[c % 2]
            free_u, free_dt = free["u"][c % 2], free["dt"][c % 2]
            wait(SP, free_u)
            x_in = dma("d_x", U[:, :, :], xT[:, c * TC:(c + 1) * TC].rearrange("(k p) t -> p k t", p=P))
            yield
            wait(SC, x_in, free_dt)
            sq = act("a_prep", T[:, :, :], U[:, :, :], ACT.Square)
            wait(PE, sq, consts)
            p = project([(mean_mat[:, :], T[:, k, :]) for k in range(KB)], True, True)
            yield
            wait(SC, p, consts, free["rinv"])
            p = free["work"] = act("a_prep", rinv[:, :], work[:, :], ACT.Ln, bias=eps_rms[:, :])
            wait(SC, p)
            r = act("a_prep", rinv[:, :], rinv[:, :], ACT.Exp, scale=-0.5)
            yield
            wait(VE, r, x_in, vec_in)
            for k in range(KB):
                p = do(VE, "v_prep", lambda e, k=k: e.scalar_tensor_tensor(
                    U[:, k, :], U[:, k, :], norm_w[:, k:k + 1], rinv[:, :], ALU.mult, ALU.mult))
            xn = free["rinv"] = p
            yield
            for m in range(KB):
                wait(PE, xn, wsel_in)
                p = project([(w_sel[:, k, m * P:(m + 1) * P], U[:, k, :]) for k in range(KB)], True, True)
                yield
                wait(SC, p, gates)
                e_m = free["work"] = act("a_prep", T[:, m, :], work[:, :], ACT.Exp,
                                         bias=neg_gate_bias[:, m:m + 1], scale=neg_gate[:, m:m + 1])
                wait(VE, e_m)
                p = do(VE, "v_prep", lambda e, m=m: e.tensor_scalar(T[:, m, :], T[:, m, :], 1.0, None, ALU.add))
                wait(VE, p)
                p = do(VE, "v_prep", lambda e, m=m: e.reciprocal(T[:, m, :], T[:, m, :]))
                last_mask = p
            yield
            wait(VE, last_mask)
            xs = do(VE, "v_prep", lambda e: e.tensor_tensor(U[:, :, :], U[:, :, :], T[:, :, :], ALU.mult))
            rows = None
            for m in (1, 2, 0):
                buf = m % 2
                wait(PE, xs, wxp_in)
                p = project([(w_xp[:, k, m * P:(m + 1) * P], U[:, k, :]) for k in range(KB)], True, True)
                yield
                wait(SC, p, free["xp_out"][buf])
                p = free["work"] = act("a_prep", xp_out[buf][:, :], work[:, :], ACT.Copy)
                if m:
                    wait(SP, p)
                    rows = free["xp_out"][buf] = dma(f"d_rows{m}", bc_scratch[c, m - 1, :, :], xp_out[buf][:, :])
                    ready[c, "B" if m == 1 else "C"] = rows
                else:
                    delta = p
            yield
            tv, te, tw = tmp
            for m in range(KB):
                wait(PE, delta, wdt_in)
                p = free["xp_out"][0] = project([(w_dt[:, m * P:(m + 1) * P], xp_out[0][:, :])], True, True)
                yield
                wait(VE, p, free["tmp"][0])
                p = free["work"] = do(VE, "v_prep", lambda e, m=m: e.tensor_scalar(
                    tv[:, :], work[:, :], dt_b[:, m:m + 1], None, ALU.add))
                wait(VE, p, free["tmp"][1])
                p = do(VE, "v_prep", lambda e: e.scalar_tensor_tensor(
                    te[:, :], tv[:, :], -1.0, tv[:, :], ALU.mult, ALU.max))
                wait(SC, p)
                ex = act("a_prep", te[:, :], te[:, :], ACT.Exp, scale=-1.0)
                wait(SC, ex, xs)
                ln = act("a_prep", T[:, m, :], te[:, :], ACT.Ln, bias=one[:, :])
                yield
                wait(VE, ex, free["tmp"][2])
                p = do(VE, "v_prep", lambda e: e.tensor_scalar(tw[:, :], te[:, :], 1.0, 1.0, ALU.add, ALU.subtract))
                wait(VE, p, ln)
                p = do(VE, "v_prep", lambda e: e.tensor_tensor(te[:, :], te[:, :], tw[:, :], ALU.subtract))
                wait(VE, p)
                p = free["tmp"][1] = free["tmp"][2] = do(VE, "v_prep", lambda e, m=m: e.tensor_tensor(
                    T[:, m, :], T[:, m, :], te[:, :], ALU.add))
                wait(VE, p)
                dt_m = free["tmp"][0] = do(VE, "v_prep", lambda e, m=m: e.scalar_tensor_tensor(
                    T[:, m, :], tv[:, :], 0.0, T[:, m, :], ALU.max, ALU.add))
            ready[c, "dt"] = dt_m
            wait(VE, dt_m)
            ready[c, "u"] = do(VE, "v_prep", lambda e: e.tensor_tensor(
                U[:, :, :], U[:, :, :], T[:, :, :], ALU.mult))
            yield

        def load_tile(src):
            slot = loaded_tiles[0] % W_RING
            loaded_tiles[0] += 1
            wait(SP, free["w_ring"][slot])
            return w_ring[:, slot, :], dma(f"d_w{slot}", w_ring[:, slot, :], src), slot

        def layernorm(v_done):
            wait(PE, v_done)
            p = project([(mean_mat[:, :], v[:, k, :]) for k in range(KB)], True, True)
            yield
            wait(VE, p)
            cen = free["work"] = do(VE, "v_fin", lambda e: e.tensor_tensor(
                v[:, :, :], v[:, :, :], over_blocks(work[:, :]), ALU.subtract))
            wait(SC, cen, free["gated"])
            sq = act("a_fin", ymod, v[:, :, :], ACT.Square)
            yield
            wait(PE, sq)
            p = free["gated"] = project([(mean_mat[:, :], ymod[:, k, :]) for k in range(KB)], True, True)
            yield
            wait(SC, p, free["rinv"])
            p = free["work"] = act("a_fin", rinv[:, :], work[:, :], ACT.Ln, bias=eps_ln[:, :])
            wait(SC, p)
            r = act("a_fin", rinv[:, :], rinv[:, :], ACT.Exp, scale=-0.5)
            yield
            wait(VE, r)
            free["rinv"] = free["v_done"] = do(VE, "v_fin", lambda e: e.tensor_tensor(
                v[:, :, :], v[:, :, :], over_blocks(rinv[:, :]), ALU.mult))

        def finish(c, ymod_done):
            for m in range(KB):
                wait(PE, ymod_done, wout_in)
                p = project([(w_out[:, k, m * P:(m + 1) * P], ymod[:, k, :]) for k in range(KB)], True, True)
                if m == KB - 1:
                    free["gated"] = p
                yield
                wait(VE, p)
                v_done = free["work"] = do(VE, "v_fin", lambda e, m=m: e.tensor_tensor(
                    v[:, m, :], v[:, m, :], work[:, :], ALU.add))
            yield from layernorm(v_done)
            x1 = free["v_done"]
            t1 = tmp[0]
            for hb in range(HB):
                tile, w_in, slot = load_tile(gu_w[hb])
                gu = tile.rearrange("p (g k m) -> p g k m", g=2, k=KB)
                wait(PE, x1, w_in)
                p = project([(gu[:, 0, k, :], v[:, k, :]) for k in range(KB)], True, True)
                yield
                wait(SC, p, free["tmp"][0])
                p = act("a_fin", t1[:, :], work[:, :], ACT.Exp, scale=-1.0)
                wait(VE, p)
                p = do(VE, "v_fin", lambda e: e.tensor_scalar(t1[:, :], t1[:, :], 1.0, None, ALU.add))
                wait(VE, p)
                p = do(VE, "v_fin", lambda e: e.reciprocal(t1[:, :], t1[:, :]))
                wait(VE, p)
                silu = free["work"] = do(VE, "v_fin", lambda e: e.tensor_tensor(
                    t1[:, :], t1[:, :], work[:, :], ALU.mult))
                p = free["w_ring"][slot] = project([(gu[:, 1, k, :], v[:, k, :]) for k in range(KB)], True, True)
                yield
                wait(VE, p, silu, free["gated"])
                hid = free["work"] = free["tmp"][0] = do(VE, "v_fin", lambda e, hb=hb: e.tensor_tensor(
                    gated[:, hb, :], t1[:, :], work[:, :], ALU.mult))
            half = HB // 2
            for m in range(KB):
                for part in range(2):
                    tile, w_in, slot = load_tile(down_w[m, part])
                    dn = tile.rearrange("p (b m) -> p b m", b=half)
                    wait(PE, w_in, hid)
                    for q in range(2):
                        lo = q * half // 2
                        p = project([(dn[:, j, :], gated[:, part * half + j, :]) for j in range(lo, lo + half // 2)],
                                    part == 0 and q == 0, part == 1 and q == 1)
                        yield
                    free["w_ring"][slot] = p
                wait(VE, p)
                v_done = free["work"] = do(VE, "v_fin", lambda e, m=m: e.tensor_tensor(
                    v[:, m, :], v[:, m, :], work[:, :], ALU.add))
            free["gated"] = p
            yield from layernorm(v_done)
            wait(SP, free["v_done"])
            free["v"] = dma("d_out", outT[:, c * TC:(c + 1) * TC].rearrange("(k p) t -> p k t", p=P), v[:, :, :])
            yield

        steps = {}
        prev_y_read = [None]

        def at(i, name):
            return steps.get((i, name))

        def z_vector(c, n, i):
            first = pool_blocks(n)
            wait(VE, at(i, "c_ps"), at(i, "scan3"), at(i - 2, "y"))
            steps[i, "z_ve"] = do(VE, "z_ve", lambda e: e.tensor_tensor(
                z[i % 2][:, first:KB, :], h[i % 2][:, first:KB, :], over_blocks(c_ps[:, :], KB - first), ALU.mult))
            if (c + 1) % PER_SEQ:
                steps[i, "carry"] = do(VE, "carry", lambda e: e.tensor_copy(carry[:, n, :], h[i % 2][:, :, TC - 1]))

        def z_gpsimd(n, i):
            blocks = pool_blocks(n)
            wait(GP, at(i, "c_row"), at(i, f"scan{blocks - 1}"), at(i - 2, "y"))
            row = c_row[:, i % ROW_RING, :]
            steps[i, "z_gp"] = do(GP, "z_gp", lambda e: e.tensor_tensor(
                z[i % 2][:, 0:blocks, :], h[i % 2][:, 0:blocks, :], over_blocks(row, blocks), ALU.mult))

        def y_sum(n, i):
            wait(PE, at(i, "z_ve"), at(i, "z_gp"), ident_done)
            if n == 0:
                wait(PE, prev_y_read[0])
            for k in range(KB):
                issue = (lambda e, k=k: e.matmul(y_ps[:, k, :], ident[:, :], z[i % 2][:, k, :],
                                                 start=(n == 0), stop=(n == N - 1)))
                if k == KB - 1:
                    steps[i, "y"] = do(PE, "y", issue)
                else:
                    quiet(PE, issue)

        def scan_step(c, n):
            i = c * N + n
            slot = i % ROW_RING
            wait(SP, at(i - ROW_RING, "b"), ready[c, "B"])
            steps[i, "b_row"] = dma(f"d_b{slot}", b_row[:, slot, :], bc_scratch[c, 0, n, :].partition_broadcast(P))
            wait(SP, at(i - ROW_RING, "z_gp"), at(i - ROW_RING, "c_ps"), ready[c, "C"])
            steps[i, "c_row"] = dma(f"d_c{slot}", c_row[:, slot, :], bc_scratch[c, 1, n, :].partition_broadcast(P))
            wait(GP, at(i, "b_row"), ready[c, "u"], at(i - 2, "scan3"))
            steps[i, "b"] = do(GP, "b", lambda e: e.tensor_tensor(
                b[i % 2][:, :, :], u[c % 2][:, :, :], over_blocks(b_row[:, slot, :]), ALU.mult))
            if n:
                z_gpsimd(n - 1, i - 1)
            wait(SC, ready[c, "dt"], A_ready)
            wait(VE, at(i, "b"), at(i - 2, "z_gp"))
            for k in range(KB):
                wait(SC, at(i if k >= 2 else i - 1, f"scan{(k - 2) % KB}"))
                steps[i, f"a{k}"] = act("a", a_ps[:, k % 2, :], dt[c % 2][:, k, :], ACT.Exp, scale=A[:, k, n:n + 1])
                if c % PER_SEQ:
                    wait(VE, at(i - N, "carry"))
                    start = carry[:, n, k:k + 1]
                else:
                    start = 0.0
                wait(VE, at(i, f"a{k}"))
                steps[i, f"scan{k}"] = do(VE, "scan", lambda e, k=k, start=start: e.tensor_tensor_scan(
                    h[i % 2][:, k, :], a_ps[:, k % 2, :], b[i % 2][:, k, :], start, ALU.mult, ALU.add))
                if k == 0 and n:
                    z_vector(c, n - 1, i - 1)
            wait(SC, at(i, "c_row"), at(i - 1, "z_ve"))
            steps[i, "c_ps"] = act("c_ps", c_ps[:, :], c_row[:, slot, :], ACT.Copy)
            if n:
                y_sum(n - 1, i - 1)

        def run(piece):
            return next(piece, "done") != "done"

        for _ in prepare(0):
            pass
        finishing = []
        for c in range(CHUNKS):
            def background():
                if finishing:
                    yield from finish(c - 1, finishing.pop())
                if c + 1 < CHUNKS:
                    yield from prepare(c + 1)
            piece = background()
            for n in range(N):
                scan_step(c, n)
                run(piece)
            last = c * N + N - 1
            z_vector(c, N - 1, last)
            z_gpsimd(N - 1, last)
            y_sum(N - 1, last)
            free["u"][c % 2] = steps[last, "b"]
            free["dt"][c % 2] = steps[last, "a3"]
            while run(piece):
                pass
            wait(SP, free["v"])
            x_again = dma("d_xv", v[:, :, :], xT[:, c * TC:(c + 1) * TC].rearrange("(k p) t -> p k t", p=P))
            wait(VE, x_again, steps[last, "y"], free["gated"])
            for k in range(KB):
                ymod_done = do(VE, "v_fin", lambda e, k=k: e.scalar_tensor_tensor(
                    ymod[:, k, :], v[:, k, :], d_skip[:, k:k + 1], y_ps[:, k, :], ALU.mult, ALU.add))
            prev_y_read[0] = ymod_done
            finishing.append(ymod_done)
        for _ in finish(CHUNKS - 1, finishing.pop()):
            pass
        wait(SP, free["v"])

        block = ctx.enter_context(nc.Block())
        for name in queues:
            def body(e, name=name):
                for issue in queues[name]:
                    issue(e)
            {"sync": block.sync, "scalar": block.scalar, "vector": block.vector,
             "gpsimd": block.gpsimd, "tensor": block.tensor}[name](body)


def kernel(L0_attn_x, L0_attn_norm_w, L0_attn_select_proj_w, L0_attn_select_proj_b, L0_attn_select_gate,
           L0_attn_x_proj_w, L0_attn_dt_proj_w, L0_attn_dt_proj_b, L0_attn_A_log, L0_attn_D_param,
           L0_attn_out_proj_w, L0_ffn_w_gate, L0_ffn_w_up, L0_ffn_w_down):
    import numpy as np
    import concourse.bacc as bacc
    from concourse.bass_utils import run_bass_kernel_spmd

    def T(w):
        return np.ascontiguousarray(np.asarray(w).T)

    vecs = np.stack([np.asarray(a).reshape(KB, P).T for a in
                     (L0_attn_norm_w, L0_attn_select_proj_b, L0_attn_select_gate, L0_attn_dt_proj_b,
                      L0_attn_D_param)], axis=1)
    gate, up = (np.asarray(w).reshape(HB, P, KB, P).transpose(0, 3, 2, 1) for w in (L0_ffn_w_gate, L0_ffn_w_up))
    gu = np.stack([gate, up], axis=2).reshape(HB, P, WT)
    down = np.asarray(L0_ffn_w_down).reshape(KB, P, 2, HB // 2, P).transpose(0, 2, 4, 3, 1).reshape(KB, 2, P, WT)
    arrays = {
        "xT": T(np.asarray(L0_attn_x).reshape(TOK, D)),
        "vecs": vecs,
        "sel_wT": T(L0_attn_select_proj_w),
        "xproj_wT": T(L0_attn_x_proj_w),
        "dt_wT": T(L0_attn_dt_proj_w),
        "out_wT": T(L0_attn_out_proj_w),
        "A_log": np.asarray(L0_attn_A_log),
        "gu_w": gu,
        "down_w": down,
    }
    arrays = {f"in_{k}": np.ascontiguousarray(a) for k, a in arrays.items()}
    nc = bacc.Bacc("TRN2", target_bir_lowering=False, num_devices=1)
    args = [nc.dram_tensor(k, a.shape, mybir.dt.from_np(a.dtype), kind="ExternalInput").ap()
            for k, a in arrays.items()]
    out = nc.dram_tensor("outT", (D, TOK), mybir.dt.float32, kind="ExternalOutput").ap()
    build(nc, *args, out)
    r = run_bass_kernel_spmd(nc, [arrays], core_ids=[0])
    return np.ascontiguousarray(r.results[0]["outT"].T).reshape(BATCH, SEQ, D)
```

```python
from contextlib import ExitStack

import concourse.bass as bass
from concourse import mybir

BATCH, SEQ, D, N, R, HID = 2, 1024, 512, 128, 128, 2048
P = 128
KB = D // P
TOK = BATCH * SEQ
TC = 512
CHUNKS = TOK // TC
PER_SEQ = SEQ // TC
HB = HID // P
XP = R + 2 * N
NV = 5
ROW_RING = 3
FFN_LATER = 4
PREP_LATER = 4
Z_RING = 3
W_RING = 2
WT = 2 * KB * P


def pool_blocks(n):
    return 1


class Counter:

    def __init__(self, sem):
        self.sem, self.value = sem, 0


def build(nc, xT, vecs, sel_wT, xproj_wT, dt_wT, out_wT, A_log, gu_w, down_w, outT):
    f32 = mybir.dt.float32
    ALU = mybir.AluOpType
    ACT = mybir.ActivationFunctionType

    ctx = ExitStack()
    with ctx:
        def sb(name, shape):
            return ctx.enter_context(nc.sbuf_tensor(name, shape, f32))

        def ps(name, shape):
            return ctx.enter_context(nc.psum_tensor(name, shape, f32))

        ident = sb("ident", [P, P])
        mean_mat = sb("mean_mat", [P, P])
        one = sb("one", [P, 1])
        minus_one = sb("minus_one", [P, 1])
        half = sb("half", [P, 1])
        eps_rms = sb("eps_rms", [P, 1])
        eps_ln = sb("eps_ln", [P, 1])
        vec = sb("vec", [P, NV, KB])
        half_gate = sb("half_gate", [P, KB])
        half_gate_bias = sb("half_gate_bias", [P, KB])
        A = sb("A", [P, KB, N])
        w_sel = sb("w_sel", [P, KB, D])
        w_xp = sb("w_xp", [P, KB, XP])
        w_dt = sb("w_dt", [P, D])
        w_out = sb("w_out", [P, KB, D])
        carry = sb("carry", [P, N, KB])
        dt = [sb(f"dt{i}", [P, KB, TC]) for i in range(2)]
        u = [sb(f"u{i}", [P, KB, TC]) for i in range(2)]
        b_row = sb("b_row", [P, ROW_RING, TC])
        c_row = sb("c_row", [P, ROW_RING, TC])
        b = [sb(f"b{i}", [P, KB, TC]) for i in range(2)]
        h = [sb(f"h{i}", [P, KB, TC]) for i in range(2)]
        z = [sb(f"z{i}", [P, KB, TC]) for i in range(Z_RING)]
        row_tmp = sb("row_tmp", [P, TC])
        xp_out = [sb(f"xp_out{i}", [P, TC]) for i in range(2)]
        t_exp = sb("t_exp", [P, TC])
        t_one = sb("t_one", [P, TC])
        t_gate = sb("t_gate", [P, TC])
        v = sb("v", [P, KB, TC])
        gated = sb("gated", [P, HB, TC])
        ymod = gated[:, 0:KB, :]
        w_ring = sb("w_ring", [P, W_RING, WT])

        y_ps = ps("y_ps", [P, KB, TC])
        a_ps = ps("a_ps", [P, 2, TC])
        c_ps = ps("c_ps", [P, TC])
        work = ps("work", [P, TC])

        bc_scratch = nc.dram_tensor("bc_scratch", [CHUNKS, 2, N, TC], f32, kind="Internal").ap()

        queues = {e: [] for e in ("sync", "scalar", "vector", "gpsimd", "tensor")}
        SP, SC, VE, GP, PE = queues.keys()
        waited = {}
        counters = {}

        def counter(name):
            if name not in counters:
                counters[name] = Counter(ctx.enter_context(nc.semaphore(name)))
            return counters[name]

        def wait(engine, *points):
            for point in points:
                if point is None:
                    continue
                c, value = point
                if waited.get((engine, c), 0) < value:
                    waited[engine, c] = value
                    queues[engine].append(lambda e, s=c.sem, n=value: e.wait_ge(s, n))

        def do(engine, name, issue, by=1):
            c = counter(name)
            c.value += by
            queues[engine].append(lambda e: issue(e).then_inc(c.sem, by))
            return c, c.value

        def quiet(engine, issue):
            queues[engine].append(lambda e: issue(e))

        def dma(name, dst, src, queue=SP):
            return do(queue, name, lambda e: e.dma_start(dst, src), 16)

        def act(name, dst, src, func, **kw):
            return do(SC, name, lambda e: e.activation(dst, src, func, **kw))

        def over_blocks(row, blocks=KB):
            return row.unsqueeze(1).to_broadcast([P, blocks, TC])

        log_table = lambda e: e.preload_act_table_set("natural_log_exp_and_others")
        quiet(SC, log_table)
        vec_in = dma("d_vec", vec[:, :, :], vecs)
        do(VE, "consts", lambda e: e.memset(mean_mat[:, :], 1.0 / D))
        do(VE, "consts", lambda e: e.memset(one[:, :], 1.0))
        do(VE, "consts", lambda e: e.memset(minus_one[:, :], -1.0))
        do(VE, "consts", lambda e: e.memset(half[:, :], 0.5))
        do(VE, "consts", lambda e: e.memset(eps_rms[:, :], 1e-6))
        consts = do(VE, "consts", lambda e: e.memset(eps_ln[:, :], 1e-5))
        zeroed = do(GP, "ident", lambda e: e.memset(ident[:, :], 0.0))
        wait(GP, zeroed)
        ident_done = do(GP, "ident", lambda e: e.affine_select(
            out=ident[:, :], in_=ident[:, :], compare_op=ALU.not_equal, fill=1.0, base=0,
            pattern=[[-1, P]], channel_multiplier=1))
        norm_w, sel_b, sel_g, dt_b, d_skip = (vec[:, i, :] for i in range(NV))
        wait(VE, vec_in)
        p = do(VE, "v_small", lambda e: e.tensor_scalar(half_gate[:, :], sel_g, 0.5, None, ALU.mult))
        wait(VE, p)
        gates = do(VE, "v_small", lambda e: e.tensor_tensor(half_gate_bias[:, :], half_gate[:, :], sel_b, ALU.mult))

        free = {"dt": [None, None], "u": [None, None], "xp_out": [None, None], "row_tmp": None,
                "t_exp": None, "t_one": None, "t_gate": None, "gated": None, "v": None,
                "w_ring": [None] * W_RING}
        loaded_tiles = [0]

        banks = [work[:, :]] + [y_ps[:, k, :] for k in range(KB)]
        bank_free = [None] * len(banks)
        usable = [len(banks)]
        taken = [0]

        def later(slots):
            for _ in range(slots):
                yield

        def take_bank():
            index = taken[0] % usable[0]
            taken[0] += 1
            wait(PE, bank_free[index])
            return index

        def project(parts, index, first=True, last=True):
            for i, (w, x) in enumerate(parts):
                s, t = first and i == 0, last and i == len(parts) - 1
                issue = (lambda e, w=w, x=x, s=s, t=t: e.matmul(banks[index], w, x, start=s, stop=t))
                if i == len(parts) - 1:
                    return do(PE, "pe_work", issue)
                quiet(PE, issue)

        def blocks_of(x):
            return [x[:, k, :] for k in range(x.shape[1])]

        def exp_and_log(src, exp_dst, log_dst, src_ready, log_free, **affine):
            wait(SC, src_ready)
            read = act("a_back", exp_dst, src, ACT.Abs, **affine)
            wait(SC, read)
            yield
            e_done = act("a_back", exp_dst, exp_dst, ACT.Exp, scale=-1.0)
            wait(SC, e_done, log_free, consts)
            log_done = act("a_back", log_dst, exp_dst, ACT.Ln, bias=one[:, :])
            return read, e_done, log_done

        def inverse_root(index, p, eps):
            wait(SC, p, consts, free["row_tmp"])
            p = act("a_back", row_tmp[:, :], banks[index], ACT.Ln, bias=eps[:, :])
            wait(SC, p)
            p = free["row_tmp"] = act("a_back", banks[index], row_tmp[:, :], ACT.Exp, scale=-0.5)
            return p

        ready, weights = {}, {}

        def load_weights():
            weights["sel"] = dma("d_wsel", w_sel[:, :, :], sel_wT.rearrange("(k p) m -> p k m", p=P))
            weights["xp"] = dma("d_wxp", w_xp[:, :, :], xproj_wT.rearrange("(k p) m -> p k m", p=P))
            weights["dt"] = dma("d_wdt", w_dt[:, :], dt_wT)
            weights["A_log"] = dma("d_alog", A[:, :, :], A_log.rearrange("(k p) n -> p k n", p=P))
            weights["out"] = dma("d_wout", w_out[:, :, :], out_wT.rearrange("(k p) m -> p k m", p=P))

        def negate_exp_A():
            wait(SC, weights["A_log"])
            p = act("a_small", A[:, :, :], A[:, :, :], ACT.Exp)
            wait(VE, p)
            weights["A"] = do(VE, "v_small", lambda e: e.tensor_scalar(A[:, :, :], A[:, :, :], -1.0, None, ALU.mult))

        def prepare(c):
            U, T = u[c % 2], dt[c % 2]
            wait(SC, free["u"][c % 2])
            x_in = dma("d_x", U[:, :, :], xT[:, c * TC:(c + 1) * TC].rearrange("(k p) t -> p k t", p=P), SC)
            yield from later(PREP_LATER)
            wait(SC, x_in, free["dt"][c % 2])
            for k in range(KB):
                sq = act("a_back", T[:, k, :], U[:, k, :], ACT.Square)
                if k % 2:
                    yield
            index = take_bank()
            wait(PE, sq, consts)
            p = project([(mean_mat[:, :], x) for x in blocks_of(T)], index)
            yield from later(PREP_LATER)
            root = inverse_root(index, p, eps_rms)
            yield
            wait(VE, root, x_in, vec_in)
            for k in range(KB):
                xn = do(VE, "v_back", lambda e, k=k, index=index: e.scalar_tensor_tensor(
                    U[:, k, :], U[:, k, :], norm_w[:, k:k + 1], banks[index], ALU.mult, ALU.mult))
                if k % 2:
                    yield
            bank_free[index] = xn
            for m in range(KB):
                index = take_bank()
                wait(PE, xn, weights["sel"])
                p = project([(w_sel[:, k, m * P:(m + 1) * P], U[:, k, :]) for k in range(KB)], index)
                yield from later(PREP_LATER)
                wait(SC, p, gates)
                p = bank_free[index] = act("a_back", T[:, m, :], banks[index], ACT.Tanh,
                                           bias=half_gate_bias[:, m:m + 1], scale=half_gate[:, m:m + 1])
            yield
            for m in range(KB):
                index = taken[0] % usable[0]
                taken[0] += 1
                wait(SC, p, bank_free[index])
                mask = act("a_back", banks[index], T[:, m, :], ACT.Identity, bias=half[:, :], scale=0.5)
                yield
                wait(VE, mask)
                xs = bank_free[index] = do(VE, "v_back", lambda e, m=m, index=index: e.tensor_tensor(
                    U[:, m, :], U[:, m, :], banks[index], ALU.mult))
                yield
            for m in (1, 2, 0):
                buf = m % 2
                index = take_bank()
                wait(PE, xs, weights["xp"])
                p = project([(w_xp[:, k, m * P:(m + 1) * P], U[:, k, :]) for k in range(KB)], index)
                yield from later(PREP_LATER)
                wait(SC, p, free["xp_out"][buf])
                p = bank_free[index] = act("a_back", xp_out[buf][:, :], banks[index], ACT.Copy)
                if m:
                    wait(SC, p)
                    ready[c, "B" if m == 1 else "C"] = free["xp_out"][buf] = \
                        dma(f"d_rows{m}", bc_scratch[c, m - 1, :, :], xp_out[buf][:, :], SC)
                else:
                    delta = p
            quiet(SC, log_table)
            for m in range(KB):
                index = take_bank()
                wait(PE, delta, weights["dt"])
                p = free["xp_out"][0] = project([(w_dt[:, m * P:(m + 1) * P], xp_out[0][:, :])], index)
                yield from later(PREP_LATER - 1)
                wait(SC, p)
                s_done = act("a_back", banks[index], banks[index], ACT.Identity, bias=dt_b[:, m:m + 1])
                wait(SC, free["t_exp"])
                _, ex, ln = yield from exp_and_log(banks[index], t_exp[:, :], T[:, m, :], s_done, xs)
                yield
                wait(SC, free["t_one"])
                p = act("a_back", t_one[:, :], t_exp[:, :], ACT.Identity, bias=one[:, :])
                wait(SC, p)
                p = act("a_back", t_one[:, :], t_one[:, :], ACT.Identity, bias=minus_one[:, :])
                yield from later(PREP_LATER)
                wait(GP, p, ln)
                p = do(GP, "g_back", lambda e: e.tensor_tensor(t_exp[:, :], t_exp[:, :], t_one[:, :], ALU.subtract))
                wait(GP, p)
                log1p = free["t_one"] = free["t_exp"] = do(GP, "g_back", lambda e, m=m: e.tensor_tensor(
                    T[:, m, :], T[:, m, :], t_exp[:, :], ALU.add))
                yield from later(PREP_LATER)
                wait(VE, log1p, s_done)
                dt_m = do(VE, "v_back", lambda e, m=m, index=index: e.scalar_tensor_tensor(
                    T[:, m, :], banks[index], 0.0, T[:, m, :], ALU.max, ALU.add))
                yield
                wait(SC, dt_m)
                p = act("a_back", banks[index], T[:, m, :], ACT.Copy)
                yield
                wait(VE, p)
                u_m = bank_free[index] = do(VE, "v_back", lambda e, m=m, index=index: e.tensor_tensor(
                    U[:, m, :], U[:, m, :], banks[index], ALU.mult))
            ready[c, "dt"], ready[c, "u"] = dt_m, u_m

        def load_tile(src):
            slot = loaded_tiles[0] % W_RING
            loaded_tiles[0] += 1
            wait(SC, free["w_ring"][slot])
            return w_ring[:, slot, :], dma(f"d_w{slot}", w_ring[:, slot, :], src, SC), slot

        def layernorm(v_done):
            index = take_bank()
            wait(PE, v_done)
            p = project([(mean_mat[:, :], x) for x in blocks_of(v)], index)
            yield from later(3)
            wait(VE, p)
            for k in range(KB):
                cen = do(VE, "v_back", lambda e, k=k, index=index: e.tensor_tensor(
                    v[:, k, :], v[:, k, :], banks[index], ALU.subtract))
                if k % 2:
                    yield
            bank_free[index] = cen
            wait(SC, cen, free["gated"])
            for k in range(KB):
                sq = act("a_back", ymod[:, k, :], v[:, k, :], ACT.Square)
                if k % 2:
                    yield
            index = take_bank()
            wait(PE, sq)
            p = free["gated"] = project([(mean_mat[:, :], x) for x in blocks_of(ymod)], index)
            yield from later(3)
            quiet(SC, log_table)
            root = inverse_root(index, p, eps_ln)
            yield
            wait(VE, root)
            for k in range(KB):
                bank_free[index] = free["v_done"] = do(VE, "v_back", lambda e, k=k, index=index: e.tensor_tensor(
                    v[:, k, :], v[:, k, :], banks[index], ALU.mult))
                if k % 2:
                    yield

        def finish(c):
            wait(VE, x_again[c], steps[c * N + N - 1, "y"], free["gated"])
            for k in range(KB):
                ymod_done = do(VE, "v_back", lambda e, k=k: e.scalar_tensor_tensor(
                    ymod[:, k, :], v[:, k, :], d_skip[:, k:k + 1], y_ps[:, k, :], ALU.mult, ALU.add))
            y_read[0] = ymod_done
            if c == CHUNKS - 1:
                usable[0] = len(banks)
                bank_free[1:] = [ymod_done] * KB
            yield
            for m in range(KB):
                index = take_bank()
                wait(PE, ymod_done, weights["out"])
                p = project([(w_out[:, k, m * P:(m + 1) * P], ymod[:, k, :]) for k in range(KB)], index)
                free["gated"] = p
                yield from later(5)
                wait(VE, p)
                v_done = bank_free[index] = do(VE, "v_back", lambda e, m=m, index=index: e.tensor_tensor(
                    v[:, m, :], v[:, m, :], banks[index], ALU.add))
            yield from layernorm(v_done)
            x1 = free["v_done"]
            next_tile = load_tile(gu_w[0])
            for hb in range(HB):
                tile, w_in, slot = next_tile
                gu = tile.rearrange("p (g k m) -> p g k m", g=2, k=KB)
                g = take_bank()
                wait(PE, x1, w_in)
                p = project([(gu[:, 0, k, :], v[:, k, :]) for k in range(KB)], g)
                yield from later(FFN_LATER)
                next_tile = load_tile(gu_w[hb + 1] if hb + 1 < HB else down_w[0, 0])
                wait(SC, p, free["t_exp"])
                th = act("a_back", t_exp[:, :], banks[g], ACT.Tanh, scale=0.5)
                yield
                wait(VE, th, free["t_gate"])
                silu2 = bank_free[g] = free["t_exp"] = do(VE, "v_back", lambda e, g=g: e.scalar_tensor_tensor(
                    t_gate[:, :], t_exp[:, :], 1.0, banks[g], ALU.add, ALU.mult))
                up = take_bank()
                p = free["w_ring"][slot] = project([(gu[:, 1, k, :], v[:, k, :]) for k in range(KB)], up)
                yield from later(FFN_LATER)
                wait(VE, p, silu2, free["gated"])
                hid = bank_free[up] = free["t_gate"] = do(VE, "v_back", lambda e, hb=hb, up=up: e.scalar_tensor_tensor(
                    gated[:, hb, :], t_gate[:, :], 0.5, banks[up], ALU.mult, ALU.mult))
            tile_blocks, quarter = HB // 2, HB // 4
            for m in range(KB):
                index = take_bank()
                for part in range(2):
                    tile, w_in, slot = next_tile
                    dn = tile.rearrange("p (b m) -> p b m", b=tile_blocks)
                    wait(PE, w_in, hid)
                    for q in range(2):
                        p = project([(dn[:, j, :], gated[:, part * tile_blocks + j, :])
                                     for j in range(q * quarter, (q + 1) * quarter)],
                                    index, first=(part == 0 and q == 0), last=(part == 1 and q == 1))
                        yield from later(5)
                        if q == 0 and (m, part) != (KB - 1, 1):
                            next_tile = load_tile(down_w[m + part, 1 - part])
                    free["w_ring"][slot] = p
                wait(VE, p)
                v_done = bank_free[index] = do(VE, "v_back", lambda e, m=m, index=index: e.tensor_tensor(
                    v[:, m, :], v[:, m, :], banks[index], ALU.add))
            free["gated"] = p
            yield from layernorm(v_done)
            yield from later(3)
            wait(SC, free["v_done"])
            free["v"] = dma("d_out", outT[:, c * TC:(c + 1) * TC].rearrange("(k p) t -> p k t", p=P), v[:, :, :], SC)

        steps = {}
        x_again, y_read = {}, [None]

        def at(i, name):
            return steps.get((i, name))

        def z_vector(c, n, i):
            first = pool_blocks(n)
            wait(VE, at(i, "c_ps"), at(i, "scan3"), at(i - Z_RING, "y"))
            steps[i, "z_ve"] = do(VE, "z_ve", lambda e: e.tensor_tensor(
                z[i % Z_RING][:, first:KB, :], h[i % 2][:, first:KB, :], over_blocks(c_ps[:, :], KB - first), ALU.mult))

        def keep_state(c, n, i):
            if (c + 1) % PER_SEQ:
                wait(SC, at(i, "scan3"))
                steps[i, "carry"] = act("carry", carry[:, n, :], h[i % 2][:, :, TC - 1], ACT.Copy)

        def z_gpsimd(n, i):
            blocks = pool_blocks(n)
            wait(GP, at(i, "c_row"), at(i, f"scan{blocks - 1}"), at(i - Z_RING, "y"))
            row = c_row[:, i % ROW_RING, :]
            steps[i, "z_gp"] = do(GP, "z_gp", lambda e: e.tensor_tensor(
                z[i % Z_RING][:, 0:blocks, :], h[i % 2][:, 0:blocks, :], over_blocks(row, blocks), ALU.mult))

        def y_sum(n, i):
            wait(PE, at(i, "z_ve"), at(i, "z_gp"), ident_done)
            if n == 0:
                wait(PE, y_read[0], *bank_free[1:])
            for k in range(KB):
                issue = (lambda e, k=k: e.matmul(y_ps[:, k, :], ident[:, :], z[i % Z_RING][:, k, :],
                                                 start=(n == 0), stop=(n == N - 1)))
                if k == KB - 1:
                    steps[i, "y"] = do(PE, "y", issue)
                else:
                    quiet(PE, issue)

        def scan_step(c, n, piece):
            i = c * N + n
            slot = i % ROW_RING
            wait(SP, at(i - ROW_RING, "b"), ready[c, "B"])
            steps[i, "b_row"] = dma(f"d_b{slot}", b_row[:, slot, :], bc_scratch[c, 0, n, :].partition_broadcast(P))
            wait(SP, at(i - ROW_RING, "z_gp"), at(i - ROW_RING, "c_ps"), ready[c, "C"])
            steps[i, "c_row"] = dma(f"d_c{slot}", c_row[:, slot, :], bc_scratch[c, 1, n, :].partition_broadcast(P))
            wait(GP, at(i, "b_row"), ready[c, "u"], at(i - 2, "scan3"))
            steps[i, "b"] = do(GP, "b", lambda e: e.tensor_tensor(
                b[i % 2][:, :, :], u[c % 2][:, :, :], over_blocks(b_row[:, slot, :]), ALU.mult))
            if n:
                z_gpsimd(n - 1, i - 1)
            wait(SC, ready[c, "dt"], weights["A"])
            wait(VE, at(i, "b"), at(i - 2, "z_gp"), at(i - 2, "carry"))
            for k in range(KB):
                wait(SC, at(i if k >= 2 else i - 1, f"scan{(k - 2) % KB}"))
                steps[i, f"a{k}"] = act("a", a_ps[:, k % 2, :], dt[c % 2][:, k, :], ACT.Exp, scale=A[:, k, n:n + 1])
                if c % PER_SEQ:
                    wait(VE, at(i - N, "carry"))
                    start = carry[:, n, k:k + 1]
                else:
                    start = 0.0
                wait(VE, at(i, f"a{k}"))
                steps[i, f"scan{k}"] = do(VE, "scan", lambda e, k=k, start=start: e.tensor_tensor_scan(
                    h[i % 2][:, k, :], a_ps[:, k % 2, :], b[i % 2][:, k, :], start, ALU.mult, ALU.add))
                if k == 0 and n:
                    z_vector(c, n - 1, i - 1)
                if k == 0 and n >= 2:
                    y_sum(n - 2, i - 2)
                if k == 1 and n:
                    keep_state(c, n - 1, i - 1)
                if k < KB - 1:
                    run(piece)
            wait(SC, at(i, "c_row"), at(i - 1, "z_ve"))
            steps[i, "c_ps"] = act("c_ps", c_ps[:, :], c_row[:, slot, :], ACT.Copy)

        def run(piece):
            return next(piece, "done") != "done"

        first = prepare(0)
        next(first)
        load_weights()
        for _ in first:
            pass
        negate_exp_A()
        usable[0] = 1
        for c in range(CHUNKS):
            def background():
                if c:
                    yield from finish(c - 1)
                if c + 1 < CHUNKS:
                    yield from prepare(c + 1)
            piece = background()
            for n in range(N):
                scan_step(c, n, piece)
            for _ in piece:
                pass
            last = c * N + N - 1
            z_vector(c, N - 1, last)
            z_gpsimd(N - 1, last)
            y_sum(N - 2, last - 1)
            y_sum(N - 1, last)
            keep_state(c, N - 1, last)
            free["u"][c % 2] = steps[last, "b"]
            free["dt"][c % 2] = steps[last, "a3"]
            wait(SP, free["v"])
            x_again[c] = dma("d_xv", v[:, :, :], xT[:, c * TC:(c + 1) * TC].rearrange("(k p) t -> p k t", p=P))
        for _ in finish(CHUNKS - 1):
            pass
        wait(SP, free["v"])

        block = ctx.enter_context(nc.Block())
        for name in queues:
            def body(e, name=name):
                for issue in queues[name]:
                    issue(e)
            {"sync": block.sync, "scalar": block.scalar, "vector": block.vector,
             "gpsimd": block.gpsimd, "tensor": block.tensor}[name](body)


def kernel(L0_attn_x, L0_attn_norm_w, L0_attn_select_proj_w, L0_attn_select_proj_b, L0_attn_select_gate,
           L0_attn_x_proj_w, L0_attn_dt_proj_w, L0_attn_dt_proj_b, L0_attn_A_log, L0_attn_D_param,
           L0_attn_out_proj_w, L0_ffn_w_gate, L0_ffn_w_up, L0_ffn_w_down):
    import numpy as np
    import concourse.bacc as bacc
    from concourse.bass_utils import run_bass_kernel_spmd

    def T(w):
        return np.ascontiguousarray(np.asarray(w).T)

    vecs = np.stack([np.asarray(a).reshape(KB, P).T for a in
                     (L0_attn_norm_w, L0_attn_select_proj_b, L0_attn_select_gate, L0_attn_dt_proj_b,
                      L0_attn_D_param)], axis=1)
    gate, up = (np.asarray(w).reshape(HB, P, KB, P).transpose(0, 3, 2, 1) for w in (L0_ffn_w_gate, L0_ffn_w_up))
    gu = np.stack([gate, up], axis=2).reshape(HB, P, WT)
    down = np.asarray(L0_ffn_w_down).reshape(KB, P, 2, HB // 2, P).transpose(0, 2, 4, 3, 1).reshape(KB, 2, P, WT)
    arrays = {
        "xT": T(np.asarray(L0_attn_x).reshape(TOK, D)),
        "vecs": vecs,
        "sel_wT": T(L0_attn_select_proj_w),
        "xproj_wT": T(L0_attn_x_proj_w),
        "dt_wT": T(L0_attn_dt_proj_w),
        "out_wT": T(L0_attn_out_proj_w),
        "A_log": np.asarray(L0_attn_A_log),
        "gu_w": gu,
        "down_w": down,
    }
    arrays = {f"in_{k}": np.ascontiguousarray(a) for k, a in arrays.items()}
    nc = bacc.Bacc("TRN2", target_bir_lowering=False, num_devices=1)
    args = [nc.dram_tensor(k, a.shape, mybir.dt.from_np(a.dtype), kind="ExternalInput").ap()
            for k, a in arrays.items()]
    out = nc.dram_tensor("outT", (D, TOK), mybir.dt.float32, kind="ExternalOutput").ap()
    build(nc, *args, out)
    r = run_bass_kernel_spmd(nc, [arrays], core_ids=[0])
    return np.ascontiguousarray(r.results[0]["outT"].T).reshape(BATCH, SEQ, D)
```

```python
from contextlib import ExitStack

import concourse.bass as bass
from concourse import mybir

BATCH, SEQ, D, N, R, HID = 2, 1024, 512, 128, 128, 2048
P = 128
KB = D // P
TOK = BATCH * SEQ
TC = 512
CHUNKS = TOK // TC
PER_SEQ = SEQ // TC
HB = HID // P
XP = R + 2 * N
NV = 5
ROW_RING = 3
FFN_LATER = 4
PREP_LATER = 4
Z_RING = 3
W_RING = 2
WT = 2 * KB * P


def pool_blocks(n):
    return 1


class Counter:

    def __init__(self, sem):
        self.sem, self.value = sem, 0


def build(nc, xT, vecs, sel_wT, xproj_wT, dt_wT, out_wT, A_log, gu_w, down_w, outT):
    f32 = mybir.dt.float32
    ALU = mybir.AluOpType
    ACT = mybir.ActivationFunctionType

    ctx = ExitStack()
    with ctx:
        def sb(name, shape):
            return ctx.enter_context(nc.sbuf_tensor(name, shape, f32))

        def ps(name, shape):
            return ctx.enter_context(nc.psum_tensor(name, shape, f32))

        ident = sb("ident", [P, P])
        mean_mat = sb("mean_mat", [P, P])
        one = sb("one", [P, 1])
        minus_one = sb("minus_one", [P, 1])
        half = sb("half", [P, 1])
        eps_rms = sb("eps_rms", [P, 1])
        eps_ln = sb("eps_ln", [P, 1])
        vec = sb("vec", [P, NV, KB])
        half_gate = sb("half_gate", [P, KB])
        half_gate_bias = sb("half_gate_bias", [P, KB])
        A = sb("A", [P, KB, N])
        w_sel = sb("w_sel", [P, KB, D])
        w_xp = sb("w_xp", [P, KB, XP])
        w_dt = sb("w_dt", [P, D])
        w_out = sb("w_out", [P, KB, D])
        carry = sb("carry", [P, N, KB])
        dt = [sb(f"dt{i}", [P, KB, TC]) for i in range(2)]
        u = [sb(f"u{i}", [P, KB, TC]) for i in range(2)]
        b_row = sb("b_row", [P, ROW_RING, TC])
        c_row = sb("c_row", [P, ROW_RING, TC])
        b = [sb(f"b{i}", [P, KB, TC]) for i in range(2)]
        h = [sb(f"h{i}", [P, KB, TC]) for i in range(2)]
        z = [sb(f"z{i}", [P, KB, TC]) for i in range(Z_RING)]
        row_tmp = sb("row_tmp", [P, TC])
        xp_out = [sb(f"xp_out{i}", [P, TC]) for i in range(2)]
        t_exp = sb("t_exp", [P, TC])
        t_one = sb("t_one", [P, TC])
        t_gate = sb("t_gate", [P, TC])
        v = sb("v", [P, KB, TC])
        gated = sb("gated", [P, HB, TC])
        ymod = gated[:, 0:KB, :]
        w_ring = sb("w_ring", [P, W_RING, WT])

        y_ps = ps("y_ps", [P, KB, TC])
        a_ps = ps("a_ps", [P, 2, TC])
        c_ps = ps("c_ps", [P, TC])
        work = ps("work", [P, TC])

        bc_scratch = nc.dram_tensor("bc_scratch", [CHUNKS, 2, N, TC], f32, kind="Internal").ap()

        queues = {e: [] for e in ("sync", "scalar", "vector", "gpsimd", "tensor")}
        SP, SC, VE, GP, PE = queues.keys()
        waited = {}
        counters = {}

        def counter(name):
            if name not in counters:
                counters[name] = Counter(ctx.enter_context(nc.semaphore(name)))
            return counters[name]

        def wait(engine, *points):
            for point in points:
                if point is None:
                    continue
                c, value = point
                if waited.get((engine, c), 0) < value:
                    waited[engine, c] = value
                    queues[engine].append(lambda e, s=c.sem, n=value: e.wait_ge(s, n))

        def do(engine, name, issue, by=1):
            c = counter(name)
            c.value += by
            queues[engine].append(lambda e: issue(e).then_inc(c.sem, by))
            return c, c.value

        def quiet(engine, issue):
            queues[engine].append(lambda e: issue(e))

        def dma(name, dst, src, queue=SP):
            return do(queue, name, lambda e: e.dma_start(dst, src), 16)

        def act(name, dst, src, func, **kw):
            return do(SC, name, lambda e: e.activation(dst, src, func, **kw))

        def over_blocks(row, blocks=KB):
            return row.unsqueeze(1).to_broadcast([P, blocks, TC])

        log_table = lambda e: e.preload_act_table_set("natural_log_exp_and_others")
        quiet(SC, log_table)
        vec_in = dma("d_vec", vec[:, :, :], vecs)
        do(VE, "consts", lambda e: e.memset(mean_mat[:, :], 1.0 / D))
        do(VE, "consts", lambda e: e.memset(one[:, :], 1.0))
        do(VE, "consts", lambda e: e.memset(minus_one[:, :], -1.0))
        do(VE, "consts", lambda e: e.memset(half[:, :], 0.5))
        do(VE, "consts", lambda e: e.memset(eps_rms[:, :], 1e-6))
        consts = do(VE, "consts", lambda e: e.memset(eps_ln[:, :], 1e-5))
        zeroed = do(GP, "ident", lambda e: e.memset(ident[:, :], 0.0))
        wait(GP, zeroed)
        ident_done = do(GP, "ident", lambda e: e.affine_select(
            out=ident[:, :], in_=ident[:, :], compare_op=ALU.not_equal, fill=1.0, base=0,
            pattern=[[-1, P]], channel_multiplier=1))
        norm_w, sel_b, sel_g, dt_b, d_skip = (vec[:, i, :] for i in range(NV))
        wait(VE, vec_in)
        p = do(VE, "v_small", lambda e: e.tensor_scalar(half_gate[:, :], sel_g, 0.5, None, ALU.mult))
        wait(VE, p)
        gates = do(VE, "v_small", lambda e: e.tensor_tensor(half_gate_bias[:, :], half_gate[:, :], sel_b, ALU.mult))

        free = {"dt": [None, None], "u": [None, None], "xp_out": [None, None], "row_tmp": None,
                "t_exp": None, "t_one": None, "t_gate": None, "gated": None, "v": None,
                "w_ring": [None] * W_RING}
        loaded_tiles = [0]

        banks = [work[:, :]] + [y_ps[:, k, :] for k in range(KB)]
        bank_free = [None] * len(banks)
        usable = [len(banks)]
        taken = [0]

        def later(slots):
            for _ in range(slots):
                yield

        def take_bank():
            index = taken[0] % usable[0]
            taken[0] += 1
            wait(PE, bank_free[index])
            return index

        def project(parts, index, moving_done, first=True, last=True):
            for i, (w, x) in enumerate(parts):
                wait(PE, moving_done[i])
                s, t = first and i == 0, last and i == len(parts) - 1
                issue = (lambda e, w=w, x=x, s=s, t=t: e.matmul(banks[index], w, x, start=s, stop=t))
                if i == len(parts) - 1:
                    return do(PE, "pe_work", issue)
                quiet(PE, issue)

        def blocks_of(x):
            return [x[:, k, :] for k in range(x.shape[1])]

        def exp_and_log(src, exp_dst, log_dst, src_ready, log_free, **affine):
            wait(SC, src_ready)
            read = act("a_back", exp_dst, src, ACT.Abs, **affine)
            wait(SC, read)
            yield
            e_done = act("a_back", exp_dst, exp_dst, ACT.Exp, scale=-1.0)
            wait(SC, e_done, log_free, consts)
            log_done = act("a_back", log_dst, exp_dst, ACT.Ln, bias=one[:, :])
            return read, e_done, log_done

        def inverse_root(index, p, eps):
            wait(SC, p, consts, free["row_tmp"])
            p = act("a_back", row_tmp[:, :], banks[index], ACT.Ln, bias=eps[:, :])
            wait(SC, p)
            p = free["row_tmp"] = act("a_back", banks[index], row_tmp[:, :], ACT.Exp, scale=-0.5)
            return p

        ready, weights = {}, {}

        def load_weights():
            weights["sel"] = dma("d_wsel", w_sel[:, :, :], sel_wT.rearrange("(k p) m -> p k m", p=P))
            weights["xp"] = dma("d_wxp", w_xp[:, :, :], xproj_wT.rearrange("(k p) m -> p k m", p=P))
            weights["dt"] = dma("d_wdt", w_dt[:, :], dt_wT)
            weights["A_log"] = dma("d_alog", A[:, :, :], A_log.rearrange("(k p) n -> p k n", p=P))
            weights["out"] = dma("d_wout", w_out[:, :, :], out_wT.rearrange("(k p) m -> p k m", p=P))

        def negate_exp_A():
            wait(SC, weights["A_log"])
            p = act("a_small", A[:, :, :], A[:, :, :], ACT.Exp)
            wait(VE, p)
            weights["A"] = do(VE, "v_small", lambda e: e.tensor_scalar(A[:, :, :], A[:, :, :], -1.0, None, ALU.mult))

        def prepare(c):
            U, T = u[c % 2], dt[c % 2]
            wait(SC, free["u"][c % 2])
            x_in = dma("d_x", U[:, :, :], xT[:, c * TC:(c + 1) * TC].rearrange("(k p) t -> p k t", p=P), SC)
            yield from later(PREP_LATER)
            wait(SC, x_in, free["dt"][c % 2])
            squares = []
            for k in range(KB):
                squares.append(act("a_back", T[:, k, :], U[:, k, :], ACT.Square))
                if k % 2:
                    yield
            index = take_bank()
            wait(PE, consts)
            p = project([(mean_mat[:, :], x) for x in blocks_of(T)], index, squares)
            yield from later(PREP_LATER)
            root = inverse_root(index, p, eps_rms)
            yield
            wait(VE, root, x_in, vec_in)
            xn = []
            for k in range(KB):
                xn.append(do(VE, "v_back", lambda e, k=k, index=index: e.scalar_tensor_tensor(
                    U[:, k, :], U[:, k, :], norm_w[:, k:k + 1], banks[index], ALU.mult, ALU.mult)))
                if k % 2:
                    yield
            bank_free[index] = xn[-1]
            for m in range(KB):
                index = take_bank()
                wait(PE, weights["sel"])
                p = project([(w_sel[:, k, m * P:(m + 1) * P], U[:, k, :]) for k in range(KB)], index, xn)
                yield from later(PREP_LATER)
                wait(SC, p, gates)
                p = bank_free[index] = act("a_back", T[:, m, :], banks[index], ACT.Tanh,
                                           bias=half_gate_bias[:, m:m + 1], scale=half_gate[:, m:m + 1])
            yield
            xs = []
            for m in range(KB):
                index = taken[0] % usable[0]
                taken[0] += 1
                wait(SC, p, bank_free[index])
                mask = act("a_back", banks[index], T[:, m, :], ACT.Identity, bias=half[:, :], scale=0.5)
                yield
                wait(VE, mask)
                bank_free[index] = do(VE, "v_back", lambda e, m=m, index=index: e.tensor_tensor(
                    U[:, m, :], U[:, m, :], banks[index], ALU.mult))
                xs.append(bank_free[index])
                yield
            for m in (1, 2, 0):
                buf = m % 2
                index = take_bank()
                wait(PE, weights["xp"])
                p = project([(w_xp[:, k, m * P:(m + 1) * P], U[:, k, :]) for k in range(KB)], index, xs)
                yield from later(PREP_LATER)
                wait(SC, p, free["xp_out"][buf])
                p = bank_free[index] = act("a_back", xp_out[buf][:, :], banks[index], ACT.Copy)
                if m:
                    wait(SC, p)
                    ready[c, "B" if m == 1 else "C"] = free["xp_out"][buf] = \
                        dma(f"d_rows{m}", bc_scratch[c, m - 1, :, :], xp_out[buf][:, :], SC)
                else:
                    delta = p
            quiet(SC, log_table)
            alone = usable[0] > 1
            small = VE if alone else GP
            for m in range(KB):
                index = take_bank()
                wait(PE, weights["dt"])
                p = free["xp_out"][0] = project([(w_dt[:, m * P:(m + 1) * P], xp_out[0][:, :])], index, [delta])
                yield from later(PREP_LATER - 1)
                wait(SC, p)
                s_done = act("a_back", banks[index], banks[index], ACT.Identity, bias=dt_b[:, m:m + 1])
                wait(SC, free["t_exp"])
                _, ex, ln = yield from exp_and_log(banks[index], t_exp[:, :], T[:, m, :], s_done, xs[-1])
                yield
                wait(SC, free["t_one"])
                p = act("a_back", t_one[:, :], t_exp[:, :], ACT.Identity, bias=one[:, :])
                wait(SC, p)
                p = act("a_back", t_one[:, :], t_one[:, :], ACT.Identity, bias=minus_one[:, :])
                yield from later(PREP_LATER)
                wait(small, p, ln)
                p = do(small, f"corr_{small}", lambda e: e.tensor_tensor(t_exp[:, :], t_exp[:, :], t_one[:, :], ALU.subtract))
                wait(small, p)
                log1p = free["t_one"] = free["t_exp"] = do(small, f"corr_{small}", lambda e, m=m: e.tensor_tensor(
                    T[:, m, :], T[:, m, :], t_exp[:, :], ALU.add))
                yield from later(PREP_LATER)
                wait(VE, log1p, s_done)
                dt_m = bank_free[index] = do(VE, "v_back", lambda e, m=m, index=index: e.scalar_tensor_tensor(
                    T[:, m, :], banks[index], 0.0, T[:, m, :], ALU.max, ALU.add))
                yield
                if alone:
                    wait(VE, dt_m)
                    u_m = do(VE, "v_back", lambda e, m=m: e.tensor_tensor(U[:, m, :], U[:, m, :], T[:, m, :], ALU.mult))
                else:
                    wait(SC, dt_m)
                    p = act("a_back", banks[index], T[:, m, :], ACT.Copy)
                    yield
                    wait(VE, p)
                    u_m = bank_free[index] = do(VE, "v_back", lambda e, m=m, index=index: e.tensor_tensor(
                        U[:, m, :], U[:, m, :], banks[index], ALU.mult))
            ready[c, "dt"], ready[c, "u"] = dt_m, u_m

        def load_tile(src):
            slot = loaded_tiles[0] % W_RING
            loaded_tiles[0] += 1
            wait(SC, free["w_ring"][slot])
            return w_ring[:, slot, :], dma(f"d_w{slot}", w_ring[:, slot, :], src, SC), slot

        def layernorm(v_done):
            index = take_bank()
            p = project([(mean_mat[:, :], x) for x in blocks_of(v)], index, v_done)
            yield from later(3)
            wait(VE, p)
            centred = []
            for k in range(KB):
                centred.append(do(VE, "v_back", lambda e, k=k, index=index: e.tensor_tensor(
                    v[:, k, :], v[:, k, :], banks[index], ALU.subtract)))
                if k % 2:
                    yield
            bank_free[index] = centred[-1]
            wait(SC, free["gated"])
            squares = []
            for k in range(KB):
                wait(SC, centred[k])
                squares.append(act("a_back", ymod[:, k, :], v[:, k, :], ACT.Square))
                if k % 2:
                    yield
            index = take_bank()
            p = free["gated"] = project([(mean_mat[:, :], x) for x in blocks_of(ymod)], index, squares)
            yield from later(3)
            quiet(SC, log_table)
            root = inverse_root(index, p, eps_ln)
            yield
            wait(VE, root)
            free["v_done"] = []
            for k in range(KB):
                bank_free[index] = do(VE, "v_back", lambda e, k=k, index=index: e.tensor_tensor(
                    v[:, k, :], v[:, k, :], banks[index], ALU.mult))
                free["v_done"].append(bank_free[index])
                if k % 2:
                    yield

        def finish(c):
            wait(VE, x_again[c], steps[c * N + N - 1, "y"], free["gated"])
            ymod_done = []
            for k in range(KB):
                ymod_done.append(do(VE, "v_back", lambda e, k=k: e.scalar_tensor_tensor(
                    ymod[:, k, :], v[:, k, :], d_skip[:, k:k + 1], y_ps[:, k, :], ALU.mult, ALU.add)))
            y_read[0] = ymod_done[-1]
            if c == CHUNKS - 1:
                usable[0] = len(banks)
                bank_free[1:] = ymod_done
            yield
            v_done = []
            for m in range(KB):
                index = take_bank()
                wait(PE, weights["out"])
                p = project([(w_out[:, k, m * P:(m + 1) * P], ymod[:, k, :]) for k in range(KB)], index, ymod_done)
                free["gated"] = p
                yield from later(5)
                wait(VE, p)
                bank_free[index] = do(VE, "v_back", lambda e, m=m, index=index: e.tensor_tensor(
                    v[:, m, :], v[:, m, :], banks[index], ALU.add))
                v_done.append(bank_free[index])
            yield from layernorm(v_done)
            x1 = free["v_done"]
            next_tile = load_tile(gu_w[0])
            hidden_done = []
            for hb in range(HB):
                tile, w_in, slot = next_tile
                gu = tile.rearrange("p (g k m) -> p g k m", g=2, k=KB)
                g = take_bank()
                wait(PE, w_in)
                p = project([(gu[:, 0, k, :], v[:, k, :]) for k in range(KB)], g, x1)
                yield from later(FFN_LATER)
                next_tile = load_tile(gu_w[hb + 1] if hb + 1 < HB else down_w[0, 0])
                wait(SC, p, free["t_exp"])
                th = act("a_back", t_exp[:, :], banks[g], ACT.Tanh, scale=0.5)
                yield
                wait(VE, th, free["t_gate"])
                silu2 = bank_free[g] = free["t_exp"] = do(VE, "v_back", lambda e, g=g: e.scalar_tensor_tensor(
                    t_gate[:, :], t_exp[:, :], 1.0, banks[g], ALU.add, ALU.mult))
                up = take_bank()
                p = free["w_ring"][slot] = project([(gu[:, 1, k, :], v[:, k, :]) for k in range(KB)], up, x1)
                yield from later(FFN_LATER)
                wait(VE, p, silu2, free["gated"])
                bank_free[up] = free["t_gate"] = do(VE, "v_back", lambda e, hb=hb, up=up: e.scalar_tensor_tensor(
                    gated[:, hb, :], t_gate[:, :], 0.5, banks[up], ALU.mult, ALU.mult))
                hidden_done.append(bank_free[up])
            v_done = []
            tile_blocks, quarter = HB // 2, HB // 4
            for m in range(KB):
                index = take_bank()
                for part in range(2):
                    tile, w_in, slot = next_tile
                    dn = tile.rearrange("p (b m) -> p b m", b=tile_blocks)
                    wait(PE, w_in)
                    for q in range(2):
                        own = range(q * quarter, (q + 1) * quarter)
                        p = project([(dn[:, j, :], gated[:, part * tile_blocks + j, :]) for j in own], index,
                                    [hidden_done[part * tile_blocks + j] for j in own],
                                    first=(part == 0 and q == 0), last=(part == 1 and q == 1))
                        yield from later(5)
                        if q == 0 and (m, part) != (KB - 1, 1):
                            next_tile = load_tile(down_w[m + part, 1 - part])
                    free["w_ring"][slot] = p
                wait(VE, p)
                bank_free[index] = do(VE, "v_back", lambda e, m=m, index=index: e.tensor_tensor(
                    v[:, m, :], v[:, m, :], banks[index], ALU.add))
                v_done.append(bank_free[index])
            free["gated"] = p
            yield from layernorm(v_done)
            yield from later(3)
            for k in range(KB):
                wait(SC, free["v_done"][k])
                rows = outT[k * P:(k + 1) * P, c * TC:(c + 1) * TC]
                free["v"] = dma("d_out", rows, v[:, k, :], SC)

        steps = {}
        x_again, y_read = {}, [None]

        def at(i, name):
            return steps.get((i, name))

        def z_vector(c, n, i):
            first = pool_blocks(n)
            wait(VE, at(i, "c_ps"), at(i, "scan3"), at(i - Z_RING, "y"))
            steps[i, "z_ve"] = do(VE, "z_ve", lambda e: e.tensor_tensor(
                z[i % Z_RING][:, first:KB, :], h[i % 2][:, first:KB, :], over_blocks(c_ps[:, :], KB - first), ALU.mult))

        def keep_state(c, n, i):
            if (c + 1) % PER_SEQ:
                wait(SC, at(i, "scan3"))
                steps[i, "carry"] = act("carry", carry[:, n, :], h[i % 2][:, :, TC - 1], ACT.Copy)

        def z_gpsimd(n, i):
            blocks = pool_blocks(n)
            wait(GP, at(i, "c_row"), at(i, f"scan{blocks - 1}"), at(i - Z_RING, "y"))
            row = c_row[:, i % ROW_RING, :]
            steps[i, "z_gp"] = do(GP, "z_gp", lambda e: e.tensor_tensor(
                z[i % Z_RING][:, 0:blocks, :], h[i % 2][:, 0:blocks, :], over_blocks(row, blocks), ALU.mult))

        def y_sum(n, i):
            wait(PE, at(i, "z_ve"), at(i, "z_gp"), ident_done)
            if n == 0:
                wait(PE, y_read[0], *bank_free[1:])
            for k in range(KB):
                issue = (lambda e, k=k: e.matmul(y_ps[:, k, :], ident[:, :], z[i % Z_RING][:, k, :],
                                                 start=(n == 0), stop=(n == N - 1)))
                if k == KB - 1:
                    steps[i, "y"] = do(PE, "y", issue)
                else:
                    quiet(PE, issue)

        def scan_step(c, n, piece):
            i = c * N + n
            slot = i % ROW_RING
            wait(SP, at(i - ROW_RING, "b"), ready[c, "B"])
            steps[i, "b_row"] = dma(f"d_b{slot}", b_row[:, slot, :], bc_scratch[c, 0, n, :].partition_broadcast(P))
            wait(SP, at(i - ROW_RING, "z_gp"), at(i - ROW_RING, "c_ps"), ready[c, "C"])
            steps[i, "c_row"] = dma(f"d_c{slot}", c_row[:, slot, :], bc_scratch[c, 1, n, :].partition_broadcast(P))
            wait(GP, at(i, "b_row"), ready[c, "u"], at(i - 2, "scan3"))
            steps[i, "b"] = do(GP, "b", lambda e: e.tensor_tensor(
                b[i % 2][:, :, :], u[c % 2][:, :, :], over_blocks(b_row[:, slot, :]), ALU.mult))
            if n:
                z_gpsimd(n - 1, i - 1)
            wait(SC, ready[c, "dt"], weights["A"])
            wait(VE, at(i, "b"), at(i - 2, "z_gp"), at(i - 2, "carry"))
            for k in range(KB):
                wait(SC, at(i if k >= 2 else i - 1, f"scan{(k - 2) % KB}"))
                steps[i, f"a{k}"] = act("a", a_ps[:, k % 2, :], dt[c % 2][:, k, :], ACT.Exp, scale=A[:, k, n:n + 1])
                if c % PER_SEQ:
                    wait(VE, at(i - N, "carry"))
                    start = carry[:, n, k:k + 1]
                else:
                    start = 0.0
                wait(VE, at(i, f"a{k}"))
                steps[i, f"scan{k}"] = do(VE, "scan", lambda e, k=k, start=start: e.tensor_tensor_scan(
                    h[i % 2][:, k, :], a_ps[:, k % 2, :], b[i % 2][:, k, :], start, ALU.mult, ALU.add))
                if k == 0 and n:
                    z_vector(c, n - 1, i - 1)
                if k == 0 and n >= 2:
                    y_sum(n - 2, i - 2)
                if k == 1 and n:
                    keep_state(c, n - 1, i - 1)
                if k < KB - 1:
                    run(piece)
            wait(SC, at(i, "c_row"), at(i - 1, "z_ve"))
            steps[i, "c_ps"] = act("c_ps", c_ps[:, :], c_row[:, slot, :], ACT.Copy)

        def run(piece):
            return next(piece, "done") != "done"

        first = prepare(0)
        next(first)
        load_weights()
        for _ in first:
            pass
        negate_exp_A()
        usable[0] = 1
        for c in range(CHUNKS):
            def background():
                if c:
                    yield from finish(c - 1)
                if c + 1 < CHUNKS:
                    yield from prepare(c + 1)
            piece = background()
            for n in range(N):
                scan_step(c, n, piece)
            for _ in piece:
                pass
            last = c * N + N - 1
            z_vector(c, N - 1, last)
            z_gpsimd(N - 1, last)
            y_sum(N - 2, last - 1)
            y_sum(N - 1, last)
            keep_state(c, N - 1, last)
            free["u"][c % 2] = steps[last, "b"]
            free["dt"][c % 2] = steps[last, "a3"]
            wait(SP, free["v"])
            x_again[c] = dma("d_xv", v[:, :, :], xT[:, c * TC:(c + 1) * TC].rearrange("(k p) t -> p k t", p=P))
        for _ in finish(CHUNKS - 1):
            pass
        wait(SP, free["v"])

        block = ctx.enter_context(nc.Block())
        for name in queues:
            def body(e, name=name):
                for issue in queues[name]:
                    issue(e)
            {"sync": block.sync, "scalar": block.scalar, "vector": block.vector,
             "gpsimd": block.gpsimd, "tensor": block.tensor}[name](body)


def kernel(L0_attn_x, L0_attn_norm_w, L0_attn_select_proj_w, L0_attn_select_proj_b, L0_attn_select_gate,
           L0_attn_x_proj_w, L0_attn_dt_proj_w, L0_attn_dt_proj_b, L0_attn_A_log, L0_attn_D_param,
           L0_attn_out_proj_w, L0_ffn_w_gate, L0_ffn_w_up, L0_ffn_w_down):
    import numpy as np
    import concourse.bacc as bacc
    from concourse.bass_utils import run_bass_kernel_spmd

    def T(w):
        return np.ascontiguousarray(np.asarray(w).T)

    vecs = np.stack([np.asarray(a).reshape(KB, P).T for a in
                     (L0_attn_norm_w, L0_attn_select_proj_b, L0_attn_select_gate, L0_attn_dt_proj_b,
                      L0_attn_D_param)], axis=1)
    gate, up = (np.asarray(w).reshape(HB, P, KB, P).transpose(0, 3, 2, 1) for w in (L0_ffn_w_gate, L0_ffn_w_up))
    gu = np.stack([gate, up], axis=2).reshape(HB, P, WT)
    down = np.asarray(L0_ffn_w_down).reshape(KB, P, 2, HB // 2, P).transpose(0, 2, 4, 3, 1).reshape(KB, 2, P, WT)
    arrays = {
        "xT": T(np.asarray(L0_attn_x).reshape(TOK, D)),
        "vecs": vecs,
        "sel_wT": T(L0_attn_select_proj_w),
        "xproj_wT": T(L0_attn_x_proj_w),
        "dt_wT": T(L0_attn_dt_proj_w),
        "out_wT": T(L0_attn_out_proj_w),
        "A_log": np.asarray(L0_attn_A_log),
        "gu_w": gu,
        "down_w": down,
    }
    arrays = {f"in_{k}": np.ascontiguousarray(a) for k, a in arrays.items()}
    nc = bacc.Bacc("TRN2", target_bir_lowering=False, num_devices=1)
    args = [nc.dram_tensor(k, a.shape, mybir.dt.from_np(a.dtype), kind="ExternalInput").ap()
            for k, a in arrays.items()]
    out = nc.dram_tensor("outT", (D, TOK), mybir.dt.float32, kind="ExternalOutput").ap()
    build(nc, *args, out)
    r = run_bass_kernel_spmd(nc, [arrays], core_ids=[0])
    return np.ascontiguousarray(r.results[0]["outT"].T).reshape(BATCH, SEQ, D)
```
